# Optimizing a Trainium2 kernel written in Bass

```python
import numpy as np
import jax
import jax.numpy as jnp

def _softmax(x, axis=-1):
    return jax.nn.softmax(x, axis=axis)

def _gelu(x):
    return jax.nn.gelu(x, approximate=True)

def _silu(x):
    return jax.nn.silu(x)

def _sigmoid(x):
    return jax.nn.sigmoid(x)

def _layernorm(x, axis=-1, eps=1e-05):
    m = jnp.mean(x, axis=axis, keepdims=True)
    v = jnp.var(x, axis=axis, keepdims=True)
    return (x - m) / jnp.sqrt(v + eps)

def _scatter_add(tgt, idx, src, axis=0):
    return tgt.at[idx].add(src)

def _segment_sum(src, seg, n):
    return jax.ops.segment_sum(src, seg, n)
kernel_name = 'mk_cond_resid_d2_seqx_r2_d85887'

def setup_inputs(seed: int=0):
    np.random.seed(seed)
    _w = jnp.asarray

    def _rec_inputs():
        import jax
        import jax.numpy as jnp
        _rk = jax.random.key(seed)
        x = -0.000125 + 0.9999 * jax.random.normal(jax.random.fold_in(_rk, 1), (32, 128, 512), jnp.float32)
        _lenS = 128 - jax.random.randint(jax.random.fold_in(_rk, 7), (32,), 0, max(1, 128 // 4) + 1, jnp.int32)
        _lenS2 = 128 - jax.random.randint(jax.random.fold_in(_rk, 8), (32,), 0, max(1, 128 // 4) + 1, jnp.int32)
        cond_1024 = -0.00493535 + 1.00056 * jax.random.normal(jax.random.fold_in(_rk, 11), (32, 512), jnp.float32)
        return (x, cond_1024)
    x, cond_1024 = _rec_inputs()

    def _L0_cond_setup():
        import jax, jax.numpy as jnp
        import numpy as np
        import math
        N, T, D, H = (64, 256, 512, 512)
        key = jax.random.key(seed)
        k1, k2, k3, k4 = jax.random.split(key, 4)
        x = jax.random.normal(k1, (N, T, D), dtype=jnp.float32)
        h0 = jax.random.normal(k2, (N, H), dtype=jnp.float32)
        Wx = jax.random.normal(k3, (D, 4 * H), dtype=jnp.float32) / math.sqrt(D)
        Wh = jax.random.normal(k4, (H, 4 * H), dtype=jnp.float32) / math.sqrt(H)
        b = jnp.zeros((4 * H,), dtype=jnp.float32)
        return {'x': x, 'h0': h0, 'Wx': Wx, 'Wh': Wh, 'b': b}
    _L0_cond_all = _L0_cond_setup()
    _L0_cond_in = {k: v for k, v in _L0_cond_all.items() if k in ('Wx', 'Wh', 'b')}
    del _L0_cond_all

    def _L1_cond_setup():
        import jax, jax.numpy as jnp
        import numpy as np
        B, T, D_IN, V_IN, E = (64, 128, 512, 512, 512)
        key = jax.random.key(seed)
        ks = jax.random.split(key, 16)
        s = 0.01
        return {'video': jax.random.normal(ks[0], (B, V_IN), jnp.float32), 'seq': jax.random.normal(ks[1], (B, T, D_IN), jnp.float32), 'W_z': jax.random.normal(ks[2], (D_IN, E), jnp.float32) * s, 'U_z': jax.random.normal(ks[3], (E, E), jnp.float32) * s, 'C_z': jax.random.normal(ks[4], (V_IN, E), jnp.float32) * s, 'b_z': jnp.zeros((E,), jnp.float32), 'W_r': jax.random.normal(ks[5], (D_IN, E), jnp.float32) * s, 'U_r': jax.random.normal(ks[6], (E, E), jnp.float32) * s, 'C_r': jax.random.normal(ks[7], (V_IN, E), jnp.float32) * s, 'b_r': jnp.zeros((E,), jnp.float32), 'W': jax.random.normal(ks[8], (D_IN, E), jnp.float32) * s, 'U': jax.random.normal(ks[9], (E, E), jnp.float32) * s, 'C': jax.random.normal(ks[10], (V_IN, E), jnp.float32) * s, 'b': jnp.zeros((E,), jnp.float32)}
    _L1_cond_all = _L1_cond_setup()
    _L1_cond_in = {k: v for k, v in _L1_cond_all.items() if k in ('W_z', 'U_z', 'C_z', 'b_z', 'W_r', 'U_r', 'C_r', 'b_r', 'W', 'U', 'C', 'b')}
    del _L1_cond_all
    return {'x': x, 'cond_1024': cond_1024, 'L0_cond_Wx': _L0_cond_in['Wx'], 'L0_cond_Wh': _L0_cond_in['Wh'], 'L0_cond_b': _L0_cond_in['b'], 'L1_cond_W_z': _L1_cond_in['W_z'], 'L1_cond_U_z': _L1_cond_in['U_z'], 'L1_cond_C_z': _L1_cond_in['C_z'], 'L1_cond_b_z': _L1_cond_in['b_z'], 'L1_cond_W_r': _L1_cond_in['W_r'], 'L1_cond_U_r': _L1_cond_in['U_r'], 'L1_cond_C_r': _L1_cond_in['C_r'], 'L1_cond_b_r': _L1_cond_in['b_r'], 'L1_cond_W': _L1_cond_in['W'], 'L1_cond_U': _L1_cond_in['U'], 'L1_cond_C': _L1_cond_in['C'], 'L1_cond_b': _L1_cond_in['b']}

def reference(x, cond_1024, L0_cond_Wx, L0_cond_Wh, L0_cond_b, L1_cond_W_z, L1_cond_U_z, L1_cond_C_z, L1_cond_b_z, L1_cond_W_r, L1_cond_U_r, L1_cond_C_r, L1_cond_b_r, L1_cond_W, L1_cond_U, L1_cond_C, L1_cond_b):
    import jax
    import jax.numpy as jnp

    def _L0_cond_ref(x, h0, Wx, Wh, b):
        import jax, jax.numpy as jnp
        import numpy as np
        import math
        N, T, D, H = (64, 256, 512, 512)
        Hdim = h0.shape[1]
        xW = jnp.einsum('ntd,dg->ntg', x, Wx) + b

        def step(carry, xw_t):
            prev_h, prev_c = carry
            a = xw_t + prev_h @ Wh
            i = jax.nn.sigmoid(a[:, :Hdim])
            f = jax.nn.sigmoid(a[:, Hdim:2 * Hdim])
            o = jax.nn.sigmoid(a[:, 2 * Hdim:3 * Hdim])
            g = jnp.tanh(a[:, 3 * Hdim:])
            next_c = f * prev_c + i * g
            next_h = o * jnp.tanh(next_c)
            return ((next_h, next_c), next_h)
        c0 = jnp.zeros_like(h0)
        _, hs = jax.lax.scan(step, (h0, c0), jnp.swapaxes(xW, 0, 1))
        return jnp.swapaxes(hs, 0, 1)

    def _L1_cond_ref(video, seq, W_z, U_z, C_z, b_z, W_r, U_r, C_r, b_r, W, U, C, b):
        import jax, jax.numpy as jnp
        import numpy as np
        B, T, D_IN, V_IN, E = (64, 128, 512, 512, 512)
        vz = video @ C_z + b_z
        vr = video @ C_r + b_r
        vh = video @ C + b
        xz = jnp.einsum('btd,de->bte', seq, W_z)
        xr = jnp.einsum('btd,de->bte', seq, W_r)
        xh = jnp.einsum('btd,de->bte', seq, W)

        def step(h, xs):
            xzt, xrt, xht = xs
            z = jax.nn.sigmoid(xzt + h @ U_z + vz)
            r = jax.nn.sigmoid(xrt + h @ U_r + vr)
            hh = jnp.tanh(xht + r * h @ U + vh)
            h_new = (1.0 - z) * h + z * hh
            return (h_new, h_new)
        h0 = jnp.zeros((seq.shape[0], U.shape[0]), seq.dtype)
        xs = (jnp.swapaxes(xz, 0, 1), jnp.swapaxes(xr, 0, 1), jnp.swapaxes(xh, 0, 1))
        _, out_t = jax.lax.scan(step, h0, xs)
        return jnp.swapaxes(out_t, 0, 1)
    x = x + _L0_cond_ref(x, cond_1024, L0_cond_Wx, L0_cond_Wh, L0_cond_b)
    x = x + _L1_cond_ref(cond_1024, x, L1_cond_W_z, L1_cond_U_z, L1_cond_C_z, L1_cond_b_z, L1_cond_W_r, L1_cond_U_r, L1_cond_C_r, L1_cond_b_r, L1_cond_W, L1_cond_U, L1_cond_C, L1_cond_b)
    return x

_drawn_inputs = setup_inputs


def setup_inputs(seed=0):
    import zlib

    import numpy as np

    out = dict(_drawn_inputs(seed))
    spreads = {'L0_cond_b': (0.0, 0.1),
     'L1_cond_b_z': (0.0, 0.8),
     'L1_cond_b_r': (0.0, 0.8),
     'L1_cond_b': (0.0, 0.1)}
    factors = {'L1_cond_W_z': 3.759,
     'L1_cond_U_z': 8.0,
     'L1_cond_C_z': 4.614,
     'L1_cond_W_r': 8.0,
     'L1_cond_U_r': 8.0,
     'L1_cond_C_r': 8.0}
    for name, (base, spread) in spreads.items():
        noise = np.random.default_rng([zlib.crc32(name.encode()), seed]).standard_normal(out[name].shape)
        drawn = base * np.exp(spread * noise) if base else spread * noise
        out[name] = jnp.asarray(drawn.astype(out[name].dtype))
    for name, factor in factors.items():
        out[name] = (out[name] * factor).astype(out[name].dtype)
    return out
```

```python
import concourse.bass as bass
from concourse import mybir
from contextlib import ExitStack


def lstm_then_gru(nc, x, cond, wx, wh, b0, w_z, u_z, c_z, b_z, w_r, u_r, c_r, b_r, w_h, u_h, c_h, b_h, out):
    f32 = mybir.dt.float32
    bf16 = mybir.dt.bfloat16
    ALU = mybir.AluOpType
    ACT = mybir.ActivationFunctionType

    B, T, D = x.shape
    P = 128
    K = D // P
    J = P // B
    G0 = wx.shape[1] // D
    G1 = 3
    LAG = 2
    U = 4
    PARTS = 3
    assert T % U == 0 and LAG < U and J == K

    def natural(a, t):
        return a[:, bass.ds(t, 1), :].rearrange("b t (j c) -> j b (t c)", j=J)

    with ExitStack() as ctx:
        def sbuf(name, shape, dt=f32):
            return ctx.enter_context(nc.sbuf_tensor(name, shape, dt))

        def psum(name, shape, dt=f32):
            return ctx.enter_context(nc.psum_tensor(name, shape, dt))

        def sem(name):
            return ctx.enter_context(nc.semaphore(name))

        wx_sb = sbuf("wx_sb", [P, K, G0 * D])
        wh_sb = sbuf("wh_sb", [P, K, G0 * D])
        w1_sb = sbuf("w1_sb", [P, K, G1, D])
        u1_sb = sbuf("u1_sb", [P, K, G1, D])
        c1_sb = sbuf("c1_sb", [P, 2, G1, D])

        ident = sbuf("ident", [P, P])
        pick = sbuf("pick", [PARTS * B, B], bf16)
        bias0 = sbuf("bias0", [P, G0 * P])
        bias1 = sbuf("bias1", [P, G1 * P])
        part0 = sbuf("part0", [P, PARTS, G0 * P], bf16)
        part1 = sbuf("part1", [P, PARTS, G1 * P], bf16)
        inj0 = sbuf("inj0", [PARTS * B, J, G0 * P], bf16)
        inj1 = sbuf("inj1", [PARTS * B, J, G1 * P], bf16)
        rest = sbuf("rest", [P, 2, G0 * P])

        x_nat = sbuf("x_nat", [P, U, P])
        xT = sbuf("xT", [P, U, P])
        hT = sbuf("hT", [P, P])
        ifo = sbuf("ifo", [P, 3 * P])
        cand0 = sbuf("cand0", [P, P])
        ig = sbuf("ig", [P, P])
        fc = sbuf("fc", [P, P])
        cell = sbuf("cell", [P, P])
        tanh_c = sbuf("tanh_c", [P, P])
        h_nat = sbuf("h_nat", [P, 2, P])
        y_nat = sbuf("y_nat", [P, U, P])
        yT = sbuf("yT", [P, 2, P])

        gT = sbuf("gT", [P, P])
        rgT = sbuf("rgT", [P, P])
        zr = sbuf("zr", [P, 2 * P])
        rg = sbuf("rg", [P, P])
        keep = sbuf("keep", [P, P])
        cand1 = sbuf("cand1", [P, P])
        zc = sbuf("zc", [P, P])
        g_nat = sbuf("g_nat", [P, 2, P])
        o_nat = sbuf("o_nat", [P, U, P])

        ps_gates = [psum(f"ps_gates{n}", [P, G0 * P]) for n in range(2)]
        ps_zr = [psum(f"ps_zr{n}", [P, 4 * P]) for n in range(2)]
        ps_hh = [psum(f"ps_hh{n}", [P, 4 * P]) for n in range(2)]
        ps_t0 = psum("ps_t0", [P, 4 * P])
        ps_t1 = psum("ps_t1", [P, 4 * P])

        wx_in = [sem(f"wx_in{k}") for k in range(K)]
        wh_in = sem("wh_in")
        w1_in = sem("w1_in")
        u1_in = sem("u1_in")
        c1_in = [sem(f"c1_in{n}") for n in range(2)]
        bias0_in = sem("bias0_in")
        bias1_in = sem("bias1_in")
        h0_in = sem("h0_in")
        x_in = [sem(f"x_in{n}") for n in range(U)]
        inj0_in = sem("inj0_in")
        inj1_in = sem("inj1_in")
        out_done = [sem(f"out_done{n}") for n in range(U)]

        zeroed = sem("zeroed")
        consts = sem("consts")
        states_zeroed = sem("states_zeroed")
        c1_used = sem("c1_used")
        bias1_sum = sem("bias1_sum")
        split = sem("split")
        parts0 = sem("parts0")
        parts1 = sem("parts1")

        xT_ps = sem("xT_ps")
        xT_sb = sem("xT_sb")
        gates_ps = sem("gates_ps")
        cand0_done = sem("cand0_done")
        ifo_done = sem("ifo_done")
        ig_done = sem("ig_done")
        fc_done = sem("fc_done")
        cell_done = sem("cell_done")
        tanh_c_done = sem("tanh_c_done")
        h_done = sem("h_done")
        hT_ps = sem("hT_ps")
        hT_sb = sem("hT_sb")
        yT_sb = sem("yT_sb")
        y_done = sem("y_done")

        zr_ps = sem("zr_ps")
        zr_done = sem("zr_done")
        rg_done = sem("rg_done")
        keep_done = sem("keep_done")
        rgT_ps = sem("rgT_ps")
        rgT_sb = sem("rgT_sb")
        hh_ps = sem("hh_ps")
        cand1_done = sem("cand1_done")
        zc_done = sem("zc_done")
        g_done = sem("g_done")
        gT_ps = sem("gT_ps")
        gT_sb = sem("gT_sb")
        o_done = sem("o_done")

        block = ctx.enter_context(nc.Block())

        def ticks(eng, tick):
            for n in range(U):
                tick(n, n, 0, True, n >= LAG, n)
            with eng.Fori(1, T // U - 1) as i:
                for n in range(U):
                    tick(U * i + n, n, i, True, True, None)
            for t in range(T - U, T + LAG):
                tick(t, t % U, t // U, t < T, True, t)

        @block.sync
        def _(sp):
            sp.dma_start(h_nat[:, 1, :], cond.rearrange("b (j c) -> j b c", j=J)).then_inc(h0_in, 16)
            sp.dma_start(x_nat[:, 0, :], natural(x, 0)).then_inc(x_in[0], 16)
            for j in range(J):
                sp.dma_start(bias0[B * j:B * j + B, :].rearrange("b (g c) -> b g c", g=G0),
                             b0.rearrange("(o g j c) -> j o g c", o=1, g=G0, j=J)[j].to_broadcast([B, G0, P])
                             ).then_inc(bias0_in, 16)
            for k in range(K):
                sp.dma_start(wx_sb[:, k, :], wx[P * k:P * k + P, :]).then_inc(wx_in[k], 16)
            sp.dma_start(wh_sb[:], wh.rearrange("(k p) n -> p k n", p=P)).then_inc(wh_in, 16)
            for n in range(1, U):
                sp.dma_start(x_nat[:, n, :], natural(x, n)).then_inc(x_in[n], 16)
            sp.wait_ge(parts0, 1)
            for q in range(PARTS):
                for j in range(J):
                    sp.dma_start(inj0[B * q:B * q + B, j, :], part0[B * j:B * j + B, q, :]).then_inc(inj0_in, 16)
            for k in range(2):
                for g, c in enumerate((c_z, c_r, c_h)):
                    sp.dma_start(c1_sb[:, k, g, :], c[P * k:P * k + P, :]).then_inc(c1_in[0], 16)
            for g, w in enumerate((w_z, w_r, w_h)):
                sp.dma_start(w1_sb[:, :, g, :], w.rearrange("(k p) n -> p k n", p=P)).then_inc(w1_in, 16)
            sp.wait_ge(c1_used, 1)
            for k in range(2):
                for g, c in enumerate((c_z, c_r, c_h)):
                    sp.dma_start(c1_sb[:, k, g, :], c[P * (k + 2):P * (k + 3), :]).then_inc(c1_in[1], 16)
            for g, u in enumerate((u_z, u_r, u_h)):
                sp.dma_start(u1_sb[:, :, g, :], u.rearrange("(k p) n -> p k n", p=P)).then_inc(u1_in, 16)
            sp.wait_ge(parts1, 1)
            for q in range(PARTS):
                for j in range(J):
                    sp.dma_start(inj1[B * q:B * q + B, j, :], part1[B * j:B * j + B, q, :]).then_inc(inj1_in, 16)

            def tick(t, n, i, has_lstm, has_gru, static):
                if has_gru:
                    s, m = t - LAG, (n - LAG) % U
                    sp.wait_ge(o_done, s + 1)
                    sp.dma_start(natural(out, s), o_nat[:, m, :]).then_inc(out_done[m], 16)
                if has_lstm and (static is None or static + U < T):
                    sp.wait_ge(y_done, t + 1)
                    sp.dma_start(x_nat[:, n, :], natural(x, t + U)).then_inc(x_in[n], 16)

            ticks(sp, tick)
            for n in range(U):
                sp.wait_ge(out_done[n], 16 * (T // U + (1 if n >= U - LAG else 0)))

        @block.gpsimd
        def _(pool):
            for m in range(U - LAG, U):
                pool.sem_inc(out_done[m], 16)
            nc.gpsimd.memset(ident[:], 0.0).then_inc(zeroed, 1)
            nc.gpsimd.memset(pick[:], 0.0).then_inc(zeroed, 1)
            pool.wait_ge(zeroed, 2)
            nc.gpsimd.affine_select(out=ident[:], in_=ident[:], compare_op=ALU.not_equal, fill=1.0, base=0,
                                    pattern=[[-1, P]], channel_multiplier=1).then_inc(consts, 1)
            for q in range(PARTS):
                pool.wait_ge(consts, 1 + q)
                nc.gpsimd.affine_select(out=pick[:], in_=pick[:], compare_op=ALU.not_equal, fill=1.0, base=-B * q,
                                        pattern=[[-1, B]], channel_multiplier=1).then_inc(consts, 1)

            def tick(t, n, i, has_lstm, has_gru, static):
                if has_gru:
                    s, m = t - LAG, (n - LAG) % U
                    pool.wait_ge(g_done, s + 1)
                    pool.wait_ge(y_done, s + 1)
                    if static is None or static >= U:
                        pool.wait_ge(out_done[m], 16 * i)
                    nc.gpsimd.tensor_tensor(o_nat[:, m, :], y_nat[:, m, :], g_nat[:, m % 2, :], ALU.add
                                            ).then_inc(o_done, 1)
                if has_lstm:
                    pool.wait_ge(h_done, t + 1)
                    if static is None or static >= U:
                        pool.wait_ge(o_done, t + 1 - U)
                    pool.wait_ge(x_in[n], 16 * (i + 1))
                    nc.gpsimd.tensor_tensor(y_nat[:, n, :], x_nat[:, n, :], h_nat[:, n % 2, :], ALU.add
                                            ).then_inc(y_done, 1)

            ticks(pool, tick)

        @block.scalar
        def _(act):
            for g, b in enumerate((b_z, b_r, b_h)):
                for j in range(J):
                    act.dma_start(bias1[B * j:B * j + B, P * g:P * g + P],
                                  b.rearrange("(o j c) -> j o c", o=1, j=J)[j].to_broadcast([B, P])
                                  ).then_inc(bias1_in, 16)

            def tick(t, n, i, has_lstm, has_gru, static):
                if has_lstm:
                    gates = ps_gates[n % 2]
                    act.wait_ge(gates_ps, t + 1)
                    if static != 0:
                        act.wait_ge(ig_done, t)
                    nc.scalar.activation(cand0[:], gates[:, 3 * P:4 * P], ACT.Tanh).then_inc(cand0_done, 1)
                    if static != 0:
                        act.wait_ge(h_done, t)
                    nc.scalar.activation(ifo[:], gates[:, 0:3 * P], ACT.Sigmoid).then_inc(ifo_done, 1)
                if has_gru:
                    s = t - LAG
                    act.wait_ge(zr_ps, s + 1)
                    if static != LAG:
                        act.wait_ge(g_done, s)
                    nc.scalar.activation(zr[:], ps_zr[n % 2][:, 0:2 * P], ACT.Sigmoid).then_inc(zr_done, 1)
                if has_lstm:
                    act.wait_ge(cell_done, t + 1)
                    nc.scalar.activation(tanh_c[:], cell[:], ACT.Tanh).then_inc(tanh_c_done, 1)
                if has_gru:
                    act.wait_ge(hh_ps, s + 1)
                    nc.scalar.activation(cand1[:], ps_hh[n % 2][:, 0:P], ACT.Tanh).then_inc(cand1_done, 1)

            ticks(act, tick)

        @block.vector
        def _(dve):
            nc.vector.memset(cell[:], 0.0).then_inc(states_zeroed, 1)
            nc.vector.memset(g_nat[:, 1, :], 0.0).then_inc(states_zeroed, 1)
            nc.vector.memset(gT[:], 0.0).then_inc(gT_sb, 1)
            steps = [0]

            def link(instruction):
                steps[0] += 1
                instruction.then_inc(split, 1)
                dve.wait_ge(split, steps[0])

            def split_parts(value, part, done, width):
                link(nc.vector.tensor_copy(part[:, 0, :], value))
                link(nc.vector.tensor_tensor(rest[:, 0, 0:width], value, part[:, 0, :], ALU.subtract))
                link(nc.vector.tensor_copy(part[:, 1, :], rest[:, 0, 0:width]))
                link(nc.vector.tensor_tensor(rest[:, 1, 0:width], rest[:, 0, 0:width], part[:, 1, :], ALU.subtract))
                nc.vector.tensor_copy(part[:, 2, :], rest[:, 1, 0:width]).then_inc(done, 1)

            dve.wait_ge(bias0_in, 16 * J)
            split_parts(bias0[:], part0, parts0, G0 * P)
            dve.wait_ge(hT_ps, 1)
            nc.vector.tensor_copy(hT[:], ps_t0[:, 0:P]).then_inc(hT_sb, 1)
            for n in range(LAG):
                dve.wait_ge(xT_ps, n + 1)
                nc.vector.tensor_copy(xT[:, n, :], ps_t0[:, 0:P]).then_inc(xT_sb, 1)
            dve.wait_ge(c1_used, 2)
            dve.wait_ge(bias1_in, 16 * G1 * J)
            link(nc.vector.tensor_tensor(bias1[:], ps_zr[0][:, 0:G1 * P], bias1[:], ALU.add))
            split_parts(bias1[:], part1, parts1, G1 * P)

            def tick(t, n, i, has_lstm, has_gru, static):
                s, m = t - LAG, (n - LAG) % U
                old_g, new_g = g_nat[:, (n + 1) % 2, :], g_nat[:, n % 2, :]
                if has_lstm:
                    if static is None or static + LAG < T:
                        dve.wait_ge(xT_ps, t + LAG + 1)
                        nc.vector.tensor_copy(xT[:, (n + LAG) % U, :], ps_t0[:, 0:P]).then_inc(xT_sb, 1)
                    dve.wait_ge(ifo_done, t + 1)
                    nc.vector.tensor_tensor(ig[:], ifo[:, 0:P], cand0[:], ALU.mult).then_inc(ig_done, 1)
                    if static == 0:
                        dve.wait_ge(states_zeroed, 2)
                    nc.vector.tensor_tensor(fc[:], ifo[:, P:2 * P], cell[:], ALU.mult).then_inc(fc_done, 1)
                    dve.wait_ge(ig_done, t + 1)
                    dve.wait_ge(fc_done, t + 1)
                    nc.vector.tensor_tensor(cell[:], ig[:], fc[:], ALU.add).then_inc(cell_done, 1)
                if has_gru:
                    dve.wait_ge(zr_done, s + 1)
                    nc.vector.tensor_tensor(rg[:], zr[:, P:2 * P], old_g, ALU.mult).then_inc(rg_done, 1)
                if has_lstm:
                    dve.wait_ge(tanh_c_done, t + 1)
                    if static is None or static >= 2:
                        dve.wait_ge(y_done, t - 1)
                    nc.vector.tensor_tensor(h_nat[:, n % 2, :], ifo[:, 2 * P:3 * P], tanh_c[:], ALU.mult
                                            ).then_inc(h_done, 1)
                if has_gru:
                    nc.vector.scalar_tensor_tensor(keep[:], zr[:, 0:P], 1.0, old_g, ALU.subtract, ALU.mult
                                                   ).then_inc(keep_done, 1)
                    dve.wait_ge(rgT_ps, s + 1)
                    nc.vector.tensor_copy(rgT[:], ps_t1[:, 0:P]).then_inc(rgT_sb, 1)
                if has_lstm:
                    dve.wait_ge(hT_ps, t + 2)
                    nc.vector.tensor_copy(hT[:], ps_t0[:, 0:P]).then_inc(hT_sb, 1)
                    dve.wait_ge(xT_sb, t + 1)
                    nc.vector.tensor_tensor(yT[:, n % 2, :], ps_t0[:, 0:P], xT[:, n, :], ALU.add).then_inc(yT_sb, 1)
                if has_gru:
                    dve.wait_ge(cand1_done, s + 1)
                    nc.vector.tensor_tensor(zc[:], zr[:, 0:P], cand1[:], ALU.mult).then_inc(zc_done, 1)
                    dve.wait_ge(zc_done, s + 1)
                    dve.wait_ge(keep_done, s + 1)
                    if static is None or static >= LAG + 2:
                        dve.wait_ge(o_done, s - 1)
                    nc.vector.tensor_tensor(new_g, zc[:], keep[:], ALU.subtract).then_inc(g_done, 1)
                    if static != T + LAG - 1:
                        dve.wait_ge(gT_ps, s + 1)
                        nc.vector.tensor_copy(gT[:], ps_t1[:, 0:P]).then_inc(gT_sb, 1)

            ticks(dve, tick)

        @block.tensor
        def _(pe):
            def lstm_product(bank, lhsT, w, k, first, last):
                for j in range(J):
                    rhs = w[:, k, :].rearrange("p (g j c) -> p j g c", g=G0, j=J)[:, j]
                    mm = nc.tensor.matmul(bank[B * j:B * j + B, :].rearrange("p (g c) -> p g c", g=G0),
                                          lhsT[:, B * k:B * k + B], rhs, start=first, stop=last)
                return mm

            def gru_product(bank, lhsT, w, g0, g1, k, last):
                for j in range(J):
                    mm = nc.tensor.matmul(bank[B * j:B * j + B, 0:P * (g1 - g0)].rearrange("p (g c) -> p g c", c=P),
                                          lhsT[:, B * k:B * k + B], w[:, k, g0:g1, P * j:P * j + P],
                                          start=False, stop=last)
                return mm

            def inject(bank, rows, c0, c1):
                for j in range(J):
                    nc.tensor.matmul(bank[B * j:B * j + B, 0:c1 - c0], pick[:], rows[:, j, c0:c1],
                                     start=True, stop=False)

            def lstm_input(n, chunks):
                if 0 in chunks:
                    inject(ps_gates[n % 2], inj0, 0, G0 * P)
                for k in chunks:
                    lstm_product(ps_gates[n % 2], xT[:, n, :], wx_sb, k, False, False)

            def gru_input(n):
                inject(ps_zr[n % 2], inj1, 0, 2 * P)
                inject(ps_hh[n % 2], inj1, 2 * P, 3 * P)
                for k in range(K):
                    gru_product(ps_zr[n % 2], yT[:, n % 2, :], w1_sb, 0, 2, k, False)
                    gru_product(ps_hh[n % 2], yT[:, n % 2, :], w1_sb, 2, 3, k, False)

            pe.wait_ge(consts, 1)
            pe.wait_ge(h0_in, 16)
            nc.tensor.transpose(ps_t0[:, 0:P], h_nat[:, 1, :], ident[:]).then_inc(hT_ps, 1)
            for n in range(LAG):
                pe.wait_ge(x_in[n], 16)
                if n == 0:
                    pe.wait_ge(hT_sb, 1)
                else:
                    pe.wait_ge(xT_sb, n)
                nc.tensor.transpose(ps_t0[:, 0:P], x_nat[:, n, :], ident[:]).then_inc(xT_ps, 1)
            pe.wait_ge(xT_sb, 1)
            pe.wait_ge(consts, 1 + PARTS)
            pe.wait_ge(inj0_in, 16 * PARTS * J)
            for k in range(K):
                pe.wait_ge(wx_in[k], 16)
                lstm_input(0, [k])
            for half in range(2):
                pe.wait_ge(c1_in[half], 16 * 2 * G1)
                for k in range(2):
                    for j in range(J):
                        kk = 2 * half + k
                        mm = nc.tensor.matmul(
                            ps_zr[0][B * j:B * j + B, 0:G1 * P].rearrange("p (g c) -> p g c", c=P),
                            hT[:, B * kk:B * kk + B], c1_sb[:, k, :, P * j:P * j + P],
                            start=(kk == 0), stop=(kk == K - 1))
                mm.then_inc(c1_used, 1)

            def tick(t, n, i, has_lstm, has_gru, static):
                s, m = t - LAG, (n - LAG) % U
                if has_lstm:
                    if static == 0:
                        pe.wait_ge(wh_in, 16)
                    pe.wait_ge(hT_sb, t + 1)
                    for k in range(K):
                        mm = lstm_product(ps_gates[n % 2], hT, wh_sb, k, False, k == K - 1)
                    mm.then_inc(gates_ps, 1)
                    if static is None or static + LAG < T:
                        pe.wait_ge(x_in[(n + LAG) % U], 16 * (i + 1 + (1 if n + LAG >= U else 0)))
                        if static == 0:
                            pe.wait_ge(xT_sb, LAG)
                        else:
                            pe.wait_ge(yT_sb, t)
                        nc.tensor.transpose(ps_t0[:, 0:P], x_nat[:, (n + LAG) % U, :], ident[:]).then_inc(xT_ps, 1)
                if has_gru:
                    if static == LAG:
                        pe.wait_ge(u1_in, 16 * G1)
                    pe.wait_ge(gT_sb, s + 1)
                    for k in range(K):
                        mm = gru_product(ps_zr[n % 2], gT, u1_sb, 0, 2, k, k == K - 1)
                    mm.then_inc(zr_ps, 1)
                ahead = has_lstm and (static is None or static + 1 < T)
                if ahead:
                    pe.wait_ge(xT_sb, t + 2)
                    if static != 0:
                        pe.wait_ge(ifo_done, t)
                    lstm_input((n + 1) % U, [0, 1])
                if has_gru:
                    pe.wait_ge(rg_done, s + 1)
                    nc.tensor.transpose(ps_t1[:, 0:P], rg[:], ident[:]).then_inc(rgT_ps, 1)
                if ahead:
                    lstm_input((n + 1) % U, [2, 3])
                if has_gru:
                    pe.wait_ge(rgT_sb, s + 1)
                    for k in range(K):
                        mm = gru_product(ps_hh[n % 2], rgT, u1_sb, 2, 3, k, k == K - 1)
                    mm.then_inc(hh_ps, 1)
                if has_lstm:
                    pe.wait_ge(h_done, t + 1)
                    if static is None or static + LAG < T:
                        pe.wait_ge(xT_sb, t + LAG + 1)
                    else:
                        pe.wait_ge(yT_sb, t)
                    nc.tensor.transpose(ps_t0[:, 0:P], h_nat[:, n % 2, :], ident[:]).then_inc(hT_ps, 1)
                if static is None or 1 <= static <= T:
                    if static == 1:
                        pe.wait_ge(w1_in, 16 * G1)
                        pe.wait_ge(inj1_in, 16 * PARTS * J)
                        pe.wait_ge(parts1, 1)
                    pe.wait_ge(yT_sb, t)
                    if static is None or static >= LAG + 1:
                        pe.wait_ge(cand1_done, s)
                    gru_input(n + 1)
                if has_gru and static != T + LAG - 1:
                    pe.wait_ge(g_done, s + 1)
                    nc.tensor.transpose(ps_t1[:, 0:P], g_nat[:, n % 2, :], ident[:]).then_inc(gT_ps, 1)

            ticks(pe, tick)


_INS = ['x', 'cond_1024', 'L0_cond_Wx', 'L0_cond_Wh', 'L0_cond_b',
        'L1_cond_W_z', 'L1_cond_U_z', 'L1_cond_C_z', 'L1_cond_b_z',
        'L1_cond_W_r', 'L1_cond_U_r', 'L1_cond_C_r', 'L1_cond_b_r',
        'L1_cond_W', 'L1_cond_U', 'L1_cond_C', 'L1_cond_b']


def kernel(**inputs):
    import numpy as _np
    import concourse.bacc as _bacc
    from concourse import mybir as _mybir
    from concourse.bass_utils import run_bass_kernel_spmd as _run

    nc = _bacc.Bacc("TRN2", target_bir_lowering=False, num_devices=1)
    arrays, args = {}, []
    for name in _INS:
        a = _np.ascontiguousarray(inputs[name])
        arrays[f"in_{name}_dram"] = a
        args.append(nc.dram_tensor(f"in_{name}_dram", a.shape, _mybir.dt.from_np(a.dtype), kind="ExternalInput").ap())
    shape = inputs['x'].shape
    out = nc.dram_tensor("out_0_dram", shape, _mybir.dt.float32, kind="ExternalOutput").ap()
    lstm_then_gru(nc, *args, out)
    r = _run(nc, [arrays], core_ids=[0])
    return r.results[0]["out_0_dram"]
```

```python
import concourse.bass as bass
from concourse import mybir
from contextlib import ExitStack


def lstm_then_gru(nc, x, cond, wx, wh, b0, w_z, u_z, c_z, b_z, w_r, u_r, c_r, b_r, w_h, u_h, c_h, b_h, out):
    f32 = mybir.dt.float32
    f16 = mybir.dt.float16
    bf16 = mybir.dt.bfloat16
    i32 = mybir.dt.int32
    ALU = mybir.AluOpType
    ACT = mybir.ActivationFunctionType
    AX = mybir.AxisListType
    RMAX = bass.bass_isa.ReduceOp.max

    B, T, D = x.shape
    P = 128
    K = D // P
    J = P // B
    G0 = wx.shape[1] // D
    G1 = 3
    GROUP = 4
    U = 2 * GROUP
    LAG = 2 * GROUP
    XA = 2 * GROUP
    SLAB = G0 * D
    XQ = B * T * D // P // SLAB
    HI, LO = 0, 1
    PASSES = [(HI, HI), (HI, LO), (LO, HI)]
    H_BEFORE = 8
    X_BEFORE = 10
    NS = 6
    assert T % U == 0 and J == K and GROUP * B == P

    EXPONENT = 0x7F800000
    TOP = 14
    LEAST = 2.0 ** -16

    def inverse_bits(n):
        return float((2 * 127 + n) << 23)

    def natural(a, t):
        return a[:, bass.ds(t, 1), :].rearrange("b t (j c) -> j b (t c)", j=J)

    with ExitStack() as ctx:
        def sbuf(name, shape, dt=f32):
            return ctx.enter_context(nc.sbuf_tensor(name, shape, dt))

        def psum(name, shape, dt=f32):
            return ctx.enter_context(nc.psum_tensor(name, shape, dt))

        def sem(name):
            return ctx.enter_context(nc.semaphore(name))

        wx2 = sbuf("wx2", [P, 2, K, G0 * D], f16)
        wh2 = sbuf("wh2", [P, 2, K, G0 * D], f16)
        w12 = sbuf("w12", [P, 2, K, G1, D], f16)
        u12 = sbuf("u12", [P, 2, K, G1, D], f16)
        stage = sbuf("stage", [P, NS * SLAB])
        HALF = G1 * K * D

        ident = sbuf("ident", [P, P])
        term0 = sbuf("term0", [P, G0, D])

        sums = sbuf("sums", [P, 2 * K + XQ + 2 * G1])
        raw = sbuf("raw", [P, 6])
        top = sbuf("top", [P, 6])
        names = ["a_wx", "a_wh", "a_x", "a_h", "a_w", "a_u", "a_y", "a_g", "r_x", "r_h", "r_y", "r_g", "work", "dummy"]
        sc = sbuf("sc", [P, len(names)])
        col = {name: sc[:, n:n + 1] for n, name in enumerate(names)}

        x_turn = sbuf("x_turn", [P, GROUP, P])
        x_nat = sbuf("x_nat", [P, GROUP, P])
        x2T = sbuf("x2T", [P, 2, 2, K, GROUP, B], f16)
        made0_a = sbuf("made0_a", [P, G0, D])
        pre0 = sbuf("pre0", [P, GROUP, G0 * P])
        h2T = sbuf("h2T", [P, 2, P], f16)
        gates = sbuf("gates", [P, G0 * P])
        ifo = gates[:, 0:3 * P]
        cand0 = sbuf("cand0", [P, P])
        ig = sbuf("ig", [P, P])
        fc = cand0
        cell = sbuf("cell", [P, P])
        tanh_c = ig
        h_nat = sbuf("h_nat", [P, 2, P])
        y_nat = sbuf("y_nat", [P, U, P])
        y2T = sbuf("y2T", [P, 2, 2, K, GROUP, B], f16)

        bias1 = y_nat[:, U - G1:U, :].rearrange("p s c -> p (s c)")

        def after(half, at, shape, dt=f32):
            n = 1
            for x_ in shape:
                n *= x_
            cols = n if dt == f32 else n // 2
            ap = stage[:, HALF * half + at:HALF * half + at + cols]
            if dt != f32:
                ap = ap.bitcast(dt)
            return (ap.rearrange("p (a b) -> p a b", a=shape[0]) if len(shape) == 2 else ap), at + cols

        made0_b, at = after(1, 0, [G0, D])
        made1_a, at = after(1, at, [G1, D])
        term1, at = after(1, at, [G1, D])
        made1_b, at = after(0, 0, [G1, D])
        pre1, at = after(0, at, [GROUP, G1 * P])
        g2T, at = after(0, at, [2, P], f16)
        rg2T, at = after(0, at, [2, P], f16)
        zr, at = after(0, at, [2 * P])
        rg, at = after(0, at, [P])
        keep, at = after(0, at, [P])
        cand1, at = after(0, at, [P])
        zc = rg
        made0 = (made0_b, made0_a)
        made1 = (made1_a, made1_b)
        g_nat = sbuf("g_nat", [P, 2, P])
        o_nat = sbuf("o_nat", [P, 2, P])
        h0T = o_nat[:, 0, :]

        ps_gates, ps_gru = (psum(f"ps_{a}", [P, 4 * P]) for a in ("gates", "gru"))
        ps_made0, ps_made1 = (psum(f"ps_{a}", [P, D]) for a in ("made0", "made1"))
        ps_x, ps_h, ps_y, ps_g = (psum(f"ps_{a}", [P, 4 * P]) for a in "xhyg")

        wx_in = [sem(f"wx_in{k}") for k in range(K)]
        wh_in = [sem(f"wh_in{k}") for k in range(K)]
        xs_in = [sem(f"xs_in{q}") for q in range(XQ)]
        w1_in = [sem(f"w1_in{g}") for g in range(G1)]
        u1_in = [sem(f"u1_in{g}") for g in range(G1)]
        c1_in = sem("c1_in")
        bias0_in = sem("bias0_in")
        bias1_in = sem("bias1_in")
        h0_in = sem("h0_in")
        x_turn_in = [sem(f"x_turn_in{n}") for n in range(GROUP)]
        x_in = [sem(f"x_in{n}") for n in range(GROUP)]
        term1_in = sem("term1_in")
        pre0_in = [sem(f"pre0_in{n}") for n in range(GROUP)]
        pre1_in = [sem(f"pre1_in{n}") for n in range(GROUP)]
        out_done = [sem(f"out_done{n}") for n in range(2)]

        zeroed = sem("zeroed")
        consts = sem("consts")
        states_zeroed = sem("states_zeroed")
        table_up = sem("table_up")
        wx_abs = sem("wx_abs")
        wh_abs = sem("wh_abs")
        x_abs = sem("x_abs")
        w1_abs = sem("w1_abs")
        u1_abs = sem("u1_abs")
        raw_done = sem("raw_done")
        top_done = sem("top_done")
        link_done = sem("link_done")
        scales0 = sem("scales0")
        scale_w = sem("scale_w")
        scale_u = sem("scale_u")
        wx_hi = sem("wx_hi")
        wx_split = sem("wx_split")
        wh_hi = sem("wh_hi")
        wh_split = sem("wh_split")
        w1_hi = sem("w1_hi")
        w1_split = sem("w1_split")
        u1_hi = sem("u1_hi")
        u1_split = sem("u1_split")
        bias1_sum = sem("bias1_sum")
        h0T_sb = sem("h0T_sb")
        cond_ps = sem("cond_ps")

        xT_ps = sem("xT_ps")
        xT_hi = sem("xT_hi")
        xT_sb = sem("xT_sb")
        gates_ps = sem("gates_ps")
        cand0_sum = sem("cand0_sum")
        ifo_sum = sem("ifo_sum")
        cand0_done = sem("cand0_done")
        ifo_done = sem("ifo_done")
        ig_done = sem("ig_done")
        fc_done = sem("fc_done")
        cell_done = sem("cell_done")
        tanh_c_done = sem("tanh_c_done")
        h_done = sem("h_done")
        hT_ps = sem("hT_ps")
        hT_hi = sem("hT_hi")
        hT_lo = sem("hT_lo")
        y_done = sem("y_done")
        yT_ps = sem("yT_ps")
        yT_hi = sem("yT_hi")
        yT_sb = sem("yT_sb")

        made0_ps = sem("made0_ps")
        made0_sb = sem("made0_sb")

        gru_ps = sem("gru_ps")
        zr_sum = sem("zr_sum")
        zr_done = sem("zr_done")
        rg_done = sem("rg_done")
        keep_done = sem("keep_done")
        rgT_ps = sem("rgT_ps")
        rgT_hi = sem("rgT_hi")
        rgT_lo = sem("rgT_lo")
        hh_ps = sem("hh_ps")
        cand1_sum = sem("cand1_sum")
        cand1_done = sem("cand1_done")
        zc_done = sem("zc_done")
        g_done = sem("g_done")
        gT_ps = sem("gT_ps")
        gT_hi = sem("gT_hi")
        gT_lo = sem("gT_lo")
        o_done = sem("o_done")

        made1_ps = sem("made1_ps")
        made1_sb = sem("made1_sb")

        block = ctx.enter_context(nc.Block())

        def ticks(eng, tick):
            for n in range(U):
                tick(n, n, 0, True, False, n)
            with eng.Fori(1, T // U - 1) as i:
                for n in range(U):
                    tick(U * i + n, n, i, True, True, None)
            for t in range(T - U, T + LAG):
                tick(t, t % U, t // U, t < T, True, t)

        def slab(q):
            return stage[:, SLAB * (q % NS):SLAB * (q % NS) + SLAB]

        def staged(half, g):
            return stage[:, HALF * half + K * D * g:HALF * half + K * D * (g + 1)].rearrange("p (k n) -> p k n", k=K)

        def to_natural(eng, pre, made, q, gates, done):
            for j in range(J):
                eng.dma_start(pre[B * j:B * j + B, q, :].rearrange("b (g c) -> b g c", g=gates),
                              made[B * q:B * q + B, :, P * j:P * j + P]).then_inc(done, 16)

        @block.sync
        def _(sp):
            sp.dma_start(h_nat[:, 1, :], cond.rearrange("b (j c) -> j b c", j=J)).then_inc(h0_in, 16)
            for k in range(K):
                sp.dma_start(slab(k), wx[P * k:P * k + P, :]).then_inc(wx_in[k], 16)
            for q in range(GROUP):
                sp.dma_start(x_turn[:, q, :], natural(x, q)).then_inc(x_turn_in[q], 16)
                sp.dma_start(x_nat[:, q, :], natural(x, q)).then_inc(x_in[q], 16)
            for k in range(K):
                if K + k >= NS:
                    sp.wait_ge(wx_split, K + k - NS + 1)
                sp.dma_start(slab(K + k), wh[P * k:P * k + P, :]).then_inc(wh_in[k], 16)
            x_flat = x.rearrange("b t d -> (b t d)").rearrange("(p n) -> p n", p=P)
            for q in range(XQ):
                before = 2 * K + q - NS
                if before < K:
                    sp.wait_ge(wx_split, before + 1)
                elif before < 2 * K:
                    sp.wait_ge(wh_split, before - K + 1)
                else:
                    sp.wait_ge(x_abs, before - 2 * K + 1)
                sp.dma_start(slab(2 * K + q), x_flat[:, SLAB * q:SLAB * q + SLAB]).then_inc(xs_in[q], 16)
            sp.wait_ge(x_abs, XQ)
            for g, c in enumerate((c_z, c_r, c_h)):
                sp.dma_start(staged(0, g), c.rearrange("(k p) n -> p k n", p=P)).then_inc(c1_in, 16)
            for g, w in enumerate((w_z, w_r, w_h)):
                sp.dma_start(staged(1, g), w.rearrange("(k p) n -> p k n", p=P)).then_inc(w1_in[g], 16)

            def turn_load(m, slot):
                sp.dma_start(x_turn[:, slot, :], natural(x, m)).then_inc(x_turn_in[slot], 16)

            for m in range(GROUP, XA):
                sp.wait_ge(xT_ps, m - GROUP + 1)
                turn_load(m, m % GROUP)
            sp.wait_ge(made0_sb, G0)
            for q in range(GROUP):
                to_natural(sp, pre0, made0_a, q, G0, pre0_in[q])

            def tick(t, n, i, has_lstm, has_gru, static):
                s, q, parity = t - LAG, n % GROUP, n // GROUP
                if has_lstm and (static is None or static + XA < T):
                    sp.wait_ge(xT_ps, t + XA - GROUP + 1)
                    turn_load(t + XA, q)
                if static == 1:
                    sp.wait_ge(cond_ps, 1)
                    for g, u in enumerate((u_z, u_r, u_h)):
                        sp.dma_start(staged(0, g), u.rearrange("(k p) n -> p k n", p=P)).then_inc(u1_in[g], 16)
                if static == 3:
                    sp.wait_ge(w1_split, G1)
                    sp.wait_ge(bias1_sum, 1)
                    for r in range(GROUP):
                        for j in range(J):
                            sp.dma_start(term1[B * r:B * r + B, :, P * j:P * j + P],
                                         bias1[B * j:B * j + B, :].rearrange("b (g c) -> b g c", g=G1)
                                         ).then_inc(term1_in, 16)
                if static == U - 1:
                    sp.wait_ge(u1_split, G1)
                if q == GROUP - 1 and (static is None or GROUP <= static < T + GROUP):
                    sp.wait_ge(made1_sb, G1 * (2 * i + parity))
                    for r in range(2):
                        to_natural(sp, pre1, made1[1 - parity], r, G1, pre1_in[r])
                if q == GROUP - 1 and (static is None or static + 1 < T):
                    sp.wait_ge(made0_sb, G0 + t + 1)
                    to_natural(sp, pre0, made0[1 - parity], 0, G0, pre0_in[0])
                if q < GROUP - 1 and has_lstm and (static is None or static >= GROUP):
                    to_natural(sp, pre0, made0[parity], q + 1, G0, pre0_in[q + 1])
                if q < 2 and has_gru:
                    sp.wait_ge(g_done, s + 1)
                    to_natural(sp, pre1, made1[parity], q + 2, G1, pre1_in[q + 2])
                if has_gru:
                    sp.wait_ge(o_done, s + 3)
                    sp.dma_start(natural(out, s), o_nat[:, n % 2, :]).then_inc(out_done[n % 2], 16)
                if has_lstm and (static is None or static + GROUP < T):
                    sp.wait_ge(y_done, t + 1)
                    sp.dma_start(x_nat[:, q, :], natural(x, t + GROUP)).then_inc(x_in[q], 16)

            ticks(sp, tick)
            for n in range(2):
                sp.wait_ge(out_done[n], 16 * (T // 2 + 1))

        @block.gpsimd
        def _(pool):
            for n in range(2):
                pool.sem_inc(out_done[n], 16)
            for n in range(GROUP):
                pool.sem_inc(pre1_in[n], 16 * J)
            pool.sem_inc(o_done, 2)
            nc.gpsimd.memset(ident[:], 0.0).then_inc(zeroed, 1)
            pool.wait_ge(zeroed, 1)
            nc.gpsimd.affine_select(out=ident[:], in_=ident[:], compare_op=ALU.not_equal, fill=1.0, base=0,
                                    pattern=[[-1, P]], channel_multiplier=1).then_inc(consts, 1)
            def all_partitions(count, c0, c1):
                pool.wait_ge(raw_done, count)
                nc.gpsimd.partition_all_reduce(top[:, c0:c1], raw[:, c0:c1], P, RMAX).then_inc(top_done, 1)

            all_partitions(1, 0, 1)
            all_partitions(2, 1, 2)
            all_partitions(3, 2, 4)

            def tick(t, n, i, has_lstm, has_gru, static):
                q = n % GROUP
                if static == 3:
                    all_partitions(4, 4, 5)
                if static == 6:
                    all_partitions(5, 5, 6)
                if has_gru:
                    s = t - LAG
                    pool.wait_ge(g_done, s + 2)
                    pool.wait_ge(y_done, s + 1)
                    pool.wait_ge(out_done[n % 2], 16 * (U // 2 * (i - 1) + n // 2 + 1))
                    nc.gpsimd.tensor_tensor(o_nat[:, n % 2, :], y_nat[:, n, :], g_nat[:, n % 2, :], ALU.add
                                            ).then_inc(o_done, 1)
                if has_lstm:
                    pool.wait_ge(h_done, t + 1)
                    if has_gru:
                        pool.wait_ge(o_done, s + 3)
                        pool.wait_ge(yT_ps, s + 1)
                    if static is not None and static == U - G1:
                        pool.wait_ge(term1_in, 16 * GROUP * J)
                    pool.wait_ge(x_in[q], 16 * (2 * i + n // GROUP + 1))
                    nc.gpsimd.tensor_tensor(y_nat[:, n, :], x_nat[:, q, :], h_nat[:, n % 2, :], ALU.add
                                            ).then_inc(y_done, 1)

            ticks(pool, tick)

        @block.scalar
        def _(act):
            act.dma_start(term0[:].rearrange("p g n -> p (g n)"),
                          b0.rearrange("(o n) -> o n", o=1).to_broadcast([P, G0 * D])).then_inc(bias0_in, 16)
            for g, b in enumerate((b_z, b_r, b_h)):
                for j in range(J):
                    act.dma_start(bias1[B * j:B * j + B, P * g:P * g + P],
                                  b.rearrange("(o j c) -> j o c", o=1, j=J)[j].to_broadcast([B, P])
                                  ).then_inc(bias1_in, 16)

            act.wait_ge(states_zeroed, 3)
            nc.scalar.activation(col["dummy"], col["dummy"], ACT.Sigmoid).then_inc(table_up, 1)

            for k in range(K):
                act.wait_ge(wx_in[k], 16)
                nc.scalar.activation(wx2[:, LO, k, :], slab(k), ACT.Abs, accum_out=sums[:, k:k + 1]
                                     ).then_inc(wx_abs, 1)
            for k in range(K):
                act.wait_ge(wh_in[k], 16)
                nc.scalar.activation(wh2[:, LO, k, :], slab(K + k), ACT.Abs, accum_out=sums[:, K + k:K + k + 1]
                                     ).then_inc(wh_abs, 1)
            for q in range(XQ):
                act.wait_ge(xs_in[q], 16)
                nc.scalar.activation(slab(2 * K + q), slab(2 * K + q), ACT.Abs,
                                     accum_out=sums[:, 2 * K + q:2 * K + q + 1]).then_inc(x_abs, 1)

            def by_k(ps):
                return ps[:, 0:P].rearrange("p (k b) -> p k b", k=K)

            act.wait_ge(scales0, 1)
            act.wait_ge(hT_ps, 1)
            nc.scalar.mul(h2T[:, HI, :], ps_h[:, 0:P], col["a_h"]).then_inc(hT_hi, 1)
            for m in range(XA):
                act.wait_ge(xT_ps, m + 1)
                nc.scalar.mul(x2T[:, m // GROUP, HI, :, m % GROUP, :], by_k((ps_x, ps_y)[m % 2]), col["a_x"]
                              ).then_inc(xT_hi, 1)

            def prepare(t):
                for t_abs, half, w2, arrived, summed, scaled, a, his, c in (
                        (2, 1, w12, w1_in, w1_abs, scale_w, "a_w", w1_hi, 2 * K + XQ),
                        (5, 0, u12, u1_in, u1_abs, scale_u, "a_u", u1_hi, 2 * K + XQ + G1)):
                    if t == t_abs:
                        for g in range(G1):
                            act.wait_ge(arrived[g], 16)
                            nc.scalar.activation(w2[:, LO, :, g, :], staged(half, g), ACT.Abs,
                                                 accum_out=sums[:, c + g:c + g + 1]).then_inc(summed, 1)
                    if t == t_abs + 1:
                        act.wait_ge(scaled, 1)
                        for g in range(G1):
                            nc.scalar.mul(w2[:, HI, :, g, :], staged(half, g), col[a]).then_inc(his, 1)

            def tick(t, n, i, has_lstm, has_gru, static):
                s, q, parity = t - LAG, n % GROUP, n // GROUP
                if static is not None:
                    prepare(static)
                if static == U - 1:
                    act.wait_ge(u1_split, G1)
                if has_gru:
                    act.wait_ge(gT_ps, s + 1)
                    nc.scalar.mul(g2T[:, HI, :], ps_g[:, 0:P], col["a_g"]).then_inc(gT_hi, 1)
                if has_lstm:
                    act.wait_ge(cand0_sum, t + 1)
                    nc.scalar.activation(cand0[:], gates[:, 3 * P:4 * P], ACT.Tanh).then_inc(cand0_done, 1)
                    act.wait_ge(ifo_sum, t + 1)
                    nc.scalar.activation(ifo, ifo, ACT.Sigmoid).then_inc(ifo_done, 1)
                if has_gru:
                    act.wait_ge(zr_sum, s + 1)
                    nc.scalar.activation(zr, zr, ACT.Sigmoid).then_inc(zr_done, 1)
                if has_lstm:
                    act.wait_ge(cell_done, t + 1)
                    nc.scalar.activation(tanh_c[:], cell[:], ACT.Tanh).then_inc(tanh_c_done, 1)
                if static is None or 1 <= static <= T:
                    act.wait_ge(yT_ps, t)
                    nc.scalar.mul(y2T[:, (n - 1) % U // GROUP, HI, :, (n - 1) % GROUP, :], by_k(ps_y), col["a_y"]
                                  ).then_inc(yT_hi, 1)
                if has_lstm and static != T - 1:
                    act.wait_ge(hT_ps, t + 2)
                    nc.scalar.mul(h2T[:, HI, :], ps_h[:, 0:P], col["a_h"]).then_inc(hT_hi, 1)
                if has_gru:
                    act.wait_ge(cand1_sum, s + 1)
                    nc.scalar.activation(cand1, cand1, ACT.Tanh).then_inc(cand1_done, 1)
                if has_lstm and (static is None or static + XA < T):
                    act.wait_ge(xT_ps, t + XA + 1)
                    nc.scalar.mul(x2T[:, parity, HI, :, q, :], by_k(ps_x), col["a_x"]).then_inc(xT_hi, 1)

            ticks(act, tick)

        @block.vector
        def _(dve):
            nc.vector.memset(cell[:], 0.0).then_inc(states_zeroed, 1)
            nc.vector.memset(g_nat[:, 1, :], 0.0).then_inc(g_done, 1)
            nc.vector.memset(col["dummy"], 0.0).then_inc(states_zeroed, 1)
            nc.vector.memset(col["a_g"], 2.0 ** TOP).then_inc(states_zeroed, 1)
            links = [0]

            def link(instruction):
                links[0] += 1
                instruction.then_inc(link_done, 1)
                dve.wait_ge(link_done, links[0])

            def factor(name, bound, n=TOP):
                link(nc.vector.tensor_scalar(col["work"], bound, LEAST, None, ALU.max))
                link(nc.vector.tensor_scalar(col["work"].bitcast(i32), col["work"].bitcast(i32), EXPONENT, None,
                                             ALU.bitwise_and))
                link(nc.vector.tensor_scalar(col[name].bitcast(i32), col["work"].bitcast(i32), -1.0, inverse_bits(n),
                                             ALU.mult, ALU.add))

            def undo(name, a, b, done=None):
                link(nc.vector.tensor_tensor(col["work"], col[a], col[b], ALU.mult))
                last = nc.vector.tensor_scalar(col[name].bitcast(i32), col["work"].bitcast(i32), -1.0, inverse_bits(0),
                                               ALU.mult, ALU.add)
                if done is None:
                    link(last)
                else:
                    last.then_inc(done, 1)

            def hi_part(hi, value, scale):
                return nc.vector.tensor_scalar(hi, value, scale, None, ALU.mult)

            def lo_part(lo, value, scale, hi):
                return nc.vector.scalar_tensor_tensor(lo, value, scale, hi, ALU.mult, ALU.subtract)

            def take_out(made, ps, term, r, done):
                nc.vector.scalar_tensor_tensor(made, ps[:], col[r], term, ALU.mult, ALU.add).then_inc(done, 1)

            def by_k(ps):
                return ps[:, 0:P].rearrange("p (k b) -> p k b", k=K)

            dve.wait_ge(h0_in, 16)
            link(nc.vector.tensor_reduce(raw[:, 3:4], h_nat[:, 1, :], AX.X, ALU.max, apply_absolute_value=True))
            dve.wait_ge(hT_ps, 1)
            nc.vector.tensor_copy(h0T, ps_h[:, 0:P]).then_inc(h0T_sb, 1)

            for n, (w2, summed, his, split, name) in enumerate(((wx2, wx_abs, wx_hi, wx_split, "a_wx"),
                                                                (wh2, wh_abs, wh_hi, wh_split, "a_wh"))):
                dve.wait_ge(summed, K)
                nc.vector.tensor_reduce(raw[:, n:n + 1], sums[:, K * n:K * n + K], AX.X, ALU.max).then_inc(raw_done, 1)
                dve.wait_ge(top_done, n + 1)
                factor(name, top[:, n:n + 1])
                for k in range(K):
                    hi_part(w2[:, HI, k, :], slab(K * n + k), col[name]).then_inc(his, 1)
                    dve.wait_ge(his, k + 1)
                    lo_part(w2[:, LO, k, :], slab(K * n + k), col[name], w2[:, HI, k, :]).then_inc(split, 1)

            dve.wait_ge(x_abs, XQ)
            nc.vector.tensor_reduce(raw[:, 2:3], sums[:, 2 * K:2 * K + XQ], AX.X, ALU.max).then_inc(raw_done, 1)
            dve.wait_ge(top_done, 3)
            factor("a_x", top[:, 2:3])
            link(nc.vector.tensor_scalar(top[:, 3:4], top[:, 3:4], 1.0, None, ALU.max))
            factor("a_h", top[:, 3:4])
            link(nc.vector.tensor_scalar(top[:, 2:3], top[:, 2:3], 1.0, None, ALU.add))
            factor("a_y", top[:, 2:3])
            undo("r_x", "a_x", "a_wx")
            undo("r_h", "a_h", "a_wh", scales0)
            dve.wait_ge(hT_hi, 1)
            lo_part(h2T[:, LO, :], ps_h[:, 0:P], col["a_h"], h2T[:, HI, :]).then_inc(hT_lo, 1)
            for m in range(XA):
                if m == GROUP:
                    dve.wait_ge(bias0_in, 16)
                    for g in range(G0):
                        dve.wait_ge(made0_ps, g + 1)
                        take_out(made0_a[:, g, :], (ps_made0, ps_made1)[g % 2], term0[:, g, :], "r_x", made0_sb)
                dve.wait_ge(xT_hi, m + 1)
                lo_part(x2T[:, m // GROUP, LO, :, m % GROUP, :], by_k((ps_x, ps_y)[m % 2]), col["a_x"],
                        x2T[:, m // GROUP, HI, :, m % GROUP, :]).then_inc(xT_sb, 1)

            def prepare(t):
                if t == 2:
                    dve.wait_ge(cond_ps, 1)
                    dve.wait_ge(bias1_in, 16 * G1 * J)
                    nc.vector.tensor_tensor(bias1, ps_gru[:, 0:G1 * P], bias1, ALU.add).then_inc(bias1_sum, 1)
                for t_split, c, half, w2, summed, scaled, a, r, other, his, split in (
                        (3, 4, 1, w12, w1_abs, scale_w, "a_w", "r_y", "a_y", w1_hi, w1_split),
                        (6, 5, 0, u12, u1_abs, scale_u, "a_u", "r_g", "a_g", u1_hi, u1_split)):
                    if t == t_split:
                        dve.wait_ge(summed, G1)
                        c0 = 2 * K + XQ + G1 * (c - 4)
                        nc.vector.tensor_reduce(raw[:, c:c + 1], sums[:, c0:c0 + G1], AX.X, ALU.max
                                                ).then_inc(raw_done, 1)
                        dve.wait_ge(top_done, c)
                        factor(a, top[:, c:c + 1])
                        undo(r, other, a, scaled)
                        for g in range(G1):
                            dve.wait_ge(his, g + 1)
                            lo_part(w2[:, LO, :, g, :], staged(half, g), col[a], w2[:, HI, :, g, :]
                                    ).then_inc(split, 1)

            def tick(t, n, i, has_lstm, has_gru, static):
                s, q, parity = t - LAG, n % GROUP, n // GROUP
                group = 2 * i + parity
                old_g, new_g = g_nat[:, (n + 1) % 2, :], g_nat[:, n % 2, :]
                if static is not None:
                    prepare(static)
                if has_gru:
                    dve.wait_ge(gT_hi, s + 1)
                    lo_part(g2T[:, LO, :], ps_g[:, 0:P], col["a_g"], g2T[:, HI, :]).then_inc(gT_lo, 1)
                if has_lstm:
                    dve.wait_ge(gates_ps, t + 1)
                    dve.wait_ge(pre0_in[q], 16 * J * (group + 1))
                    nc.vector.scalar_tensor_tensor(gates[:, 3 * P:4 * P], ps_gates[:, 3 * P:4 * P], col["r_h"],
                                                   pre0[:, q, 3 * P:4 * P], ALU.mult, ALU.add).then_inc(cand0_sum, 1)
                    nc.vector.scalar_tensor_tensor(ifo, ps_gates[:, 0:3 * P], col["r_h"],
                                                   pre0[:, q, 0:3 * P], ALU.mult, ALU.add).then_inc(ifo_sum, 1)
                    dve.wait_ge(ifo_done, t + 1)
                    nc.vector.tensor_tensor(ig[:], ifo[:, 0:P], cand0[:], ALU.mult).then_inc(ig_done, 1)
                    if static == 0:
                        dve.wait_ge(states_zeroed, 3)
                    dve.wait_ge(ig_done, t + 1)
                    nc.vector.tensor_tensor(fc[:], ifo[:, P:2 * P], cell[:], ALU.mult).then_inc(fc_done, 1)
                    dve.wait_ge(fc_done, t + 1)
                    nc.vector.tensor_tensor(cell[:], ig[:], fc[:], ALU.add).then_inc(cell_done, 1)
                if has_gru:
                    dve.wait_ge(gru_ps, s + 1)
                    dve.wait_ge(pre1_in[q], 16 * J * group)
                    dve.wait_ge(g_done, s + 1)
                    nc.vector.scalar_tensor_tensor(zr, ps_gru[:, 0:2 * P], col["r_g"], pre1[:, q, 0:2 * P],
                                                   ALU.mult, ALU.add).then_inc(zr_sum, 1)
                if has_lstm:
                    dve.wait_ge(tanh_c_done, t + 1)
                    if static is None or static >= 2:
                        dve.wait_ge(y_done, t - 1)
                    nc.vector.tensor_tensor(h_nat[:, n % 2, :], ifo[:, 2 * P:3 * P], tanh_c[:], ALU.mult
                                            ).then_inc(h_done, 1)
                if has_gru:
                    dve.wait_ge(zr_done, s + 1)
                    nc.vector.tensor_tensor(rg, zr[:, P:2 * P], old_g, ALU.mult).then_inc(rg_done, 1)
                    nc.vector.scalar_tensor_tensor(keep, zr[:, 0:P], 1.0, old_g, ALU.subtract, ALU.mult
                                                   ).then_inc(keep_done, 1)
                    dve.wait_ge(rgT_ps, s + 1)
                    hi_part(rg2T[:, HI, :], ps_g[:, 0:P], col["a_g"]).then_inc(rgT_hi, 1)
                    dve.wait_ge(rgT_hi, s + 1)
                    lo_part(rg2T[:, LO, :], ps_g[:, 0:P], col["a_g"], rg2T[:, HI, :]).then_inc(rgT_lo, 1)
                if static is None or 1 <= static <= T:
                    m = (n - 1) % U
                    dve.wait_ge(yT_hi, t)
                    lo_part(y2T[:, m // GROUP, LO, :, m % GROUP, :], by_k(ps_y), col["a_y"],
                            y2T[:, m // GROUP, HI, :, m % GROUP, :]).then_inc(yT_sb, 1)
                if has_lstm and static != T - 1:
                    dve.wait_ge(hT_hi, t + 2)
                    lo_part(h2T[:, LO, :], ps_h[:, 0:P], col["a_h"], h2T[:, HI, :]).then_inc(hT_lo, 1)
                if has_lstm and (static is None or static + GROUP < T):
                    dve.wait_ge(made0_ps, G0 + t + 1)
                    if static == GROUP:
                        dve.wait_ge(w1_split, G1)
                    for r in range(GROUP):
                        dve.wait_ge(pre0_in[r], 16 * J * (1 if static is not None and static < GROUP else group))
                    take_out(made0[1 - parity][:, q, :], ps_made0, term0[:, q, :], "r_x", made0_sb)
                if has_gru:
                    dve.wait_ge(hh_ps, s + 1)
                    nc.vector.scalar_tensor_tensor(cand1, ps_gru[:, 2 * P:3 * P], col["r_g"],
                                                   pre1[:, q, 2 * P:3 * P], ALU.mult, ALU.add).then_inc(cand1_sum, 1)
                    dve.wait_ge(cand1_done, s + 1)
                    nc.vector.tensor_tensor(zc, zr[:, 0:P], cand1, ALU.mult).then_inc(zc_done, 1)
                    dve.wait_ge(zc_done, s + 1)
                    dve.wait_ge(keep_done, s + 1)
                    dve.wait_ge(o_done, s + 1)
                    nc.vector.tensor_tensor(new_g, zc, keep, ALU.subtract).then_inc(g_done, 1)
                if has_lstm and (static is None or static + XA < T):
                    dve.wait_ge(xT_hi, t + XA + 1)
                    lo_part(x2T[:, parity, LO, :, q, :], by_k(ps_x), col["a_x"], x2T[:, parity, HI, :, q, :]
                            ).then_inc(xT_sb, 1)
                if q < G1 and (static is None or GROUP <= static < T + GROUP):
                    dve.wait_ge(made1_ps, G1 * (group - 1) + q + 1)
                    if static == GROUP:
                        dve.wait_ge(term1_in, 16 * GROUP * J)
                    if static is None or static >= 2 * GROUP:
                        for r in range(GROUP):
                            dve.wait_ge(pre1_in[r], 16 * J * (group - 1))
                    take_out(made1[1 - parity][:, q, :], ps_made1, term1[:, q, :], "r_y", made1_sb)

            ticks(dve, tick)

        @block.tensor
        def _(pe):
            steps = [(a, b, k) for a, b in PASSES for k in range(K)]

            def recurrent(bank, lhsT, w, his, los, count, first=0, last=len(steps)):
                if first == 0:
                    pe.wait_ge(his, count)
                for a, b, k in steps[first:last]:
                    if a == LO and k == 0:
                        pe.wait_ge(los, count)
                    for j in range(J):
                        mm = nc.tensor.matmul(bank[B * j:B * j + B, :].rearrange("p (g c) -> p g c", c=P),
                                              lhsT[:, a, B * k:B * k + B], w(b, k, j),
                                              start=(a, b, k) == steps[0], stop=(a, b, k) == steps[-1])
                return mm

            def lstm_weights(b, k, j):
                return wh2[:, b, k, :].rearrange("p (g j c) -> p j g c", g=G0, j=J)[:, j]

            def gru_weights(g0, g1):
                return lambda b, k, j: u12[:, b, k, g0:g1, P * j:P * j + P]

            def lstm_input(bank, parity, g, first, last):
                for a, b, k in steps[first:last]:
                    mm = nc.tensor.matmul(bank[:], x2T[:, parity, a, k].rearrange("p t b -> p (t b)"),
                                          wx2[:, b, k, D * g:D * g + D],
                                          start=(a, b, k) == steps[0], stop=(a, b, k) == steps[-1])
                return mm

            def gru_input(parity, g):
                for a, b, k in steps:
                    mm = nc.tensor.matmul(ps_made1[:], y2T[:, parity, a, k].rearrange("p t b -> p (t b)"),
                                          w12[:, b, k, g, :],
                                          start=(a, b, k) == steps[0], stop=(a, b, k) == steps[-1])
                return mm

            pe.wait_ge(consts, 1)
            pe.wait_ge(h0_in, 16)
            nc.tensor.transpose(ps_h[:, 0:P], h_nat[:, 1, :], ident[:]).then_inc(hT_ps, 1)
            for m in range(XA):
                if m == GROUP:
                    pe.wait_ge(wx_split, K)
                    for g in range(G0):
                        if g >= 2:
                            pe.wait_ge(made0_sb, g - 1)
                        pe.wait_ge(xT_sb, GROUP)
                        lstm_input((ps_made0, ps_made1)[g % 2], 0, g, 0, len(steps)).then_inc(made0_ps, 1)
                pe.wait_ge(x_turn_in[m % GROUP], 16 * (m // GROUP + 1))
                if m >= 2:
                    pe.wait_ge(xT_sb, m - 1)
                nc.tensor.transpose((ps_x, ps_y)[m % 2][:, 0:P], x_turn[:, m % GROUP, :], ident[:]).then_inc(xT_ps, 1)

            def tick(t, n, i, has_lstm, has_gru, static):
                s, q, parity = t - LAG, n % GROUP, n // GROUP
                if has_lstm:
                    if static == 0:
                        pe.wait_ge(wh_split, K)
                    recurrent(ps_gates, h2T, lstm_weights, hT_hi, hT_lo, t + 1, 0, H_BEFORE)
                if has_gru:
                    pe.wait_ge(g_done, s + 1)
                    nc.tensor.transpose(ps_g[:, 0:P], g_nat[:, (n + 1) % 2, :], ident[:]).then_inc(gT_ps, 1)
                if has_lstm:
                    recurrent(ps_gates, h2T, lstm_weights, hT_hi, hT_lo, t + 1, H_BEFORE).then_inc(gates_ps, 1)
                if static == U - 1:
                    pe.wait_ge(u1_split, G1)
                if static == 1:
                    pe.wait_ge(c1_in, 16 * G1)
                    pe.wait_ge(h0T_sb, 1)
                    for k in range(K):
                        for j in range(J):
                            mm = nc.tensor.matmul(
                                ps_gru[B * j:B * j + B, 0:G1 * P].rearrange("p (g c) -> p g c", c=P),
                                h0T[:, B * k:B * k + B],
                                stage[:, 0:HALF].rearrange("p (g k n) -> p k g n", g=G1, k=K)[:, k, :, P * j:P * j + P],
                                start=(k == 0), stop=(k == K - 1))
                    mm.then_inc(cond_ps, 1)
                if has_gru:
                    recurrent(ps_gru[:, 0:2 * P], g2T, gru_weights(0, 2), gT_hi, gT_lo, s + 1).then_inc(gru_ps, 1)
                ahead = has_lstm and (static is None or static + GROUP < T)
                if ahead:
                    pe.wait_ge(made0_sb, G0 + t)
                    pe.wait_ge(xT_sb, t - q + 2 * GROUP)
                    lstm_input(ps_made0, 1 - parity, q, 0, X_BEFORE)
                if has_gru:
                    pe.wait_ge(rg_done, s + 1)
                    nc.tensor.transpose(ps_g[:, 0:P], rg, ident[:]).then_inc(rgT_ps, 1)
                if static is None or 1 <= static <= T:
                    pe.wait_ge(y_done, t)
                    if static == 1:
                        pe.wait_ge(xT_sb, XA)
                    else:
                        pe.wait_ge(yT_sb, t - 1)
                    nc.tensor.transpose(ps_y[:, 0:P], y_nat[:, (n - 1) % U, :], ident[:]).then_inc(yT_ps, 1)
                if has_lstm and static != T - 1:
                    pe.wait_ge(h_done, t + 1)
                    nc.tensor.transpose(ps_h[:, 0:P], h_nat[:, n % 2, :], ident[:]).then_inc(hT_ps, 1)
                if ahead:
                    lstm_input(ps_made0, 1 - parity, q, X_BEFORE, len(steps)).then_inc(made0_ps, 1)
                if has_gru:
                    recurrent(ps_gru[:, 2 * P:3 * P], rg2T, gru_weights(2, 3), rgT_hi, rgT_lo, s + 1
                              ).then_inc(hh_ps, 1)
                if has_lstm and (static is None or static + XA < T):
                    pe.wait_ge(x_turn_in[q], 16 * (2 * i + parity + XA // GROUP + 1))
                    pe.wait_ge(xT_sb, t + XA)
                    nc.tensor.transpose(ps_x[:, 0:P], x_turn[:, q, :], ident[:]).then_inc(xT_ps, 1)
                if q < G1 and (static is None or GROUP <= static < T + GROUP):
                    if static == GROUP:
                        pe.wait_ge(w1_split, G1)
                    else:
                        pe.wait_ge(made1_sb, G1 * (2 * i + parity - 1) + q)
                    pe.wait_ge(yT_sb, t - q)
                    gru_input(1 - parity, q).then_inc(made1_ps, 1)

            ticks(pe, tick)


_INS = ['x', 'cond_1024', 'L0_cond_Wx', 'L0_cond_Wh', 'L0_cond_b',
        'L1_cond_W_z', 'L1_cond_U_z', 'L1_cond_C_z', 'L1_cond_b_z',
        'L1_cond_W_r', 'L1_cond_U_r', 'L1_cond_C_r', 'L1_cond_b_r',
        'L1_cond_W', 'L1_cond_U', 'L1_cond_C', 'L1_cond_b']


def kernel(**inputs):
    import numpy as _np
    import concourse.bacc as _bacc
    from concourse import mybir as _mybir
    from concourse.bass_utils import run_bass_kernel_spmd as _run

    nc = _bacc.Bacc("TRN2", target_bir_lowering=False, num_devices=1)
    arrays, args = {}, []
    for name in _INS:
        a = _np.ascontiguousarray(inputs[name])
        arrays[f"in_{name}_dram"] = a
        args.append(nc.dram_tensor(f"in_{name}_dram", a.shape, _mybir.dt.from_np(a.dtype), kind="ExternalInput").ap())
    shape = inputs['x'].shape
    out = nc.dram_tensor("out_0_dram", shape, _mybir.dt.float32, kind="ExternalOutput").ap()
    lstm_then_gru(nc, *args, out)
    r = _run(nc, [arrays], core_ids=[0])
    return r.results[0]["out_0_dram"]
```
